# Optimizing a Trainium2 kernel written in Bass

```python
import numpy as np
import jax
import jax.numpy as jnp

def _softmax(x, axis=-1):
    return jax.nn.softmax(x, axis=axis)
def _gelu(x):
    return jax.nn.gelu(x, approximate=True)
def _silu(x):
    return jax.nn.silu(x)
def _sigmoid(x):
    return jax.nn.sigmoid(x)
def _layernorm(x, axis=-1, eps=1e-5):
    m = jnp.mean(x, axis=axis, keepdims=True)
    v = jnp.var(x, axis=axis, keepdims=True)
    return (x - m) / jnp.sqrt(v + eps)
def _scatter_add(tgt, idx, src, axis=0):
    return tgt.at[idx].add(src)
def _segment_sum(src, seg, n):
    return jax.ops.segment_sum(src, seg, n)

kernel_name = 'mk_adj_preln_d1_adj_256_38f256'

def setup_inputs(seed: int = 0):
    np.random.seed(seed)
    _w = jnp.asarray
    def _rec_inputs():
        import jax
        import jax.numpy as jnp
        _gk = jax.random.key(seed)
        x = -0.0005207 + 1.001 * jax.random.normal(jax.random.fold_in(_gk, 1), (8192, 256), jnp.float32)
        _w = (1.0 + jnp.arange(8192, dtype=jnp.float32)) ** -0.5
        _w = _w / _w.mean()
        _pij = jnp.clip(0.000488281 * _w[:, None] * _w[None, :], 0.0, 1.0)
        _a = jax.random.uniform(jax.random.fold_in(_gk, 2), (8192, 8192)) < _pij
        _a = jnp.logical_or(_a, jnp.eye(8192, dtype=bool))
        _af = _a.astype(jnp.float32)
        adj = _af
        return x, adj
    x, adj = _rec_inputs()
    def _L0_gnn_setup():
        import jax, jax.numpy as jnp
        import numpy as np
        N = 8192
        F = 256
        NEG_INF = -9000000000000000.0
        ALPHA = 0.2
        THRESH = 1e-06
        key = jax.random.key(seed)
        k1, k2, k3, k4 = jax.random.split(key, 4)
        x = jax.random.normal(k1, (N, F), jnp.float32)
        h0 = jax.random.normal(k2, (N, F), jnp.float32)
        limit = float(np.sqrt(6.0 / (2 * F + 1)) * 1.414)
        a = jax.random.uniform(k3, (2 * F, 1), jnp.float32, -limit, limit)
        temp = jnp.zeros((5,), jnp.float32)
        adj = jax.random.bernoulli(k4, 0.005, (N, N)).astype(jnp.float32)
        adj = jnp.maximum(adj, jnp.eye(N, dtype=jnp.float32))
        return {'x': x, 'h0': h0, 'a': a, 'temp': temp, 'adj': adj, 'l': 1}
    _L0_gnn_all = _L0_gnn_setup()
    _L0_gnn_in = {k: v for k, v in _L0_gnn_all.items() if k in ('h0', 'a', 'temp', )}
    del _L0_gnn_all

    return {
        "x": x,
        "adj": adj,
        "L0_gnn_h0": _L0_gnn_in["h0"],
        "L0_gnn_a": _L0_gnn_in["a"],
        "L0_gnn_temp": _L0_gnn_in["temp"],
    }

def reference(x, adj, L0_gnn_h0, L0_gnn_a, L0_gnn_temp):
    import jax
    import jax.numpy as jnp
    def _L0_gnn_ref(x, h0, a, temp, adj, l):
        import jax, jax.numpy as jnp
        import numpy as np
        N = 8192
        F = 256
        NEG_INF = -9000000000000000.0
        ALPHA = 0.2
        THRESH = 1e-06
        Fdim = x.shape[1]
        feat_1 = x @ a[:Fdim]
        feat_2 = x @ a[Fdim:]
        e = jax.nn.leaky_relu(feat_1 + feat_2.T, ALPHA)
        att = jnp.where(adj > 0, e, NEG_INF)
        U = jax.nn.softmax(att, axis=1)
        P = 0.5 * U
        prop_u = U @ x
        rowsum = jnp.sum(U * P, axis=1)
        coe = jax.nn.sigmoid(temp)
        xi = x * rowsum[:, None]
        feat_odd = prop_u - xi
        feat_even = x + prop_u - xi
        feat = coe[2] * feat_odd + (1.0 - coe[2]) * feat_even
        sgn = jnp.sign(feat)
        mod = jnp.abs(feat)
        mod = jnp.where(mod > THRESH, mod - THRESH, 0.0)
        feat = mod * sgn
        pu = U @ feat
        feat_odd2 = feat - coe[3] * pu
        feat_even2 = pu + feat_odd2 * rowsum[:, None]
        feat_odd2 = coe[0] * feat_odd2 + (1.0 - coe[0]) * h0
        out = coe[1] * feat_even2 + (1.0 - coe[1]) * feat_odd2
        return out

    h = jnp.maximum(_layernorm(x, axis=-1), 0.0)
    x = x + _L0_gnn_ref(h, L0_gnn_h0, L0_gnn_a, L0_gnn_temp, adj, 1)
    return x


_drawn_inputs = setup_inputs


def setup_inputs(seed=0):
    import zlib

    import numpy as np

    out = dict(_drawn_inputs(seed))
    spreads = {'L0_gnn_temp': (0.0, 0.8)}
    factors = {}
    for name, (base, spread) in spreads.items():
        noise = np.random.default_rng([zlib.crc32(name.encode()), seed]).standard_normal(out[name].shape)
        drawn = base * np.exp(spread * noise) if base else spread * noise
        out[name] = jnp.asarray(drawn.astype(out[name].dtype))
    for name, factor in factors.items():
        out[name] = (out[name] * factor).astype(out[name].dtype)
    return out
```

```python
import concourse.bass as bass
from concourse import mybir
from contextlib import ExitStack

fp32 = mybir.dt.float32
i32 = mybir.dt.int32
ALU = mybir.AluOpType
ACT = mybir.ActivationFunctionType
AX = mybir.AxisListType


def adj_preln_kernel(nc, x, adj, h0, a, temp, out):
    N, F = x.shape
    P = 128
    NT = N // P
    AUG = F + 8
    COL_F2, COL_F1 = F, F + 1
    GT = 8
    NG = NT // GT
    CW = 1024
    CB = CW // P
    CP = N // CW // 2
    NEG = 9.0e15
    ALPHA = 0.2
    THRESH = 1e-6
    EPS = 1e-5

    ctx = ExitStack()
    with ctx:
        def sb(name, shape, dt=fp32):
            return ctx.enter_context(nc.sbuf_tensor(name, shape, dt))

        def pb(name, shape, dt=fp32):
            return ctx.enter_context(nc.psum_tensor(name, shape, dt))

        def sem(name):
            return ctx.enter_context(nc.semaphore(name))

        haug_d = nc.dram_tensor("haug_d", (N, AUG), fp32).ap()
        feat_d = nc.dram_tensor("feat_d", (N, F), fp32).ap()
        f2_d = nc.dram_tensor("f2_d", (NT, P), fp32).ap()
        pt_d = nc.dram_tensor("pt_d", (NT, P, N), fp32).ap()

        ident = sb("ident", [P, P])
        zeros = sb("zeros", [P, P])
        a_row = sb("a_row", [P, 2 * F])
        temp_b = sb("temp_b", [P, 5])
        coe = sb("coe", [P, 5])
        one_m = sb("one_m", [P, 5])
        one_c0 = sb("one_c0", [P, 2])
        F1 = sb("F1", [P, NT])
        F2 = sb("F2", [P, NT])
        INVZ = sb("INVZ", [P, NT])
        ROWS = sb("ROWS", [P, NT])
        LIST = sb("LIST", [1, NT], i32)
        COUNT = sb("COUNT", [1, 1], i32)

        R = sb("R", [P, 13 * 1024])
        W2 = sb("W2", [P, 2, N])
        X = R[:, 0:2 * GT * F].rearrange("p (u b f) -> p u b f", u=2, b=GT)
        HO = 2 * GT * F
        H = R[:, HO:HO + 2 * GT * AUG].rearrange("p (u b f) -> p u b f", u=2, b=GT)
        SC = R[:, 0:2 * CW].rearrange("p (u c) -> p u c", u=2)
        PC = R[:, 2 * CW:4 * CW].rearrange("p (u c) -> p u c", u=2)
        PT = R[:, 4 * CW:6 * CW].rearrange("p (u c) -> p u c", u=2)
        HB = R[:, 6 * CW:6 * CW + 2 * CB * AUG].rearrange("p (u b f) -> p u b f", u=2, b=CB)
        FB = R[:, 6 * CW:6 * CW + 2 * CB * F].rearrange("p (u b f) -> p u b f", u=2, b=CB)
        EO = 6 * CW + 2 * CB * AUG
        HT = R[:, EO:EO + AUG]
        A = W2[:, 0, :]
        F2B = W2[:, 1, :]

        st = sb("st", [P, GT, 6])
        mv = sb("mv", [P, 5, GT])
        sm = sb("sm", [P, 6, GT])
        jnk = sb("jnk", [P, 2 * GT, F], mybir.dt.bfloat16)
        f2t = sb("f2t", [NT, P])
        dsm = sb("dsm", [P, 16])
        Zc = sb("Zc", [P, 2 * CP])
        Qc = sb("Qc", [P, 2 * CP])
        T0 = sb("T0", [P, F])
        T1 = sb("T1", [P, F])
        T2 = sb("T2", [P, F])
        XT = sb("XT", [P, F])
        OT = sb("OT", [P, F])
        H0T = sb("H0T", [P, F])
        FT = sb("FT", [P, F])

        TP = [pb(f"TP{u}", [P, CW]) for u in range(2)]
        ACC = pb("ACC", [P, F])
        MISC = pb("MISC", [P, P])

        class Steps:

            def __init__(self, eng, s, base, per):
                self.eng, self.s, self.base, self.per, self.k = eng, s, base, per, 0

            def __call__(self, ins):
                self.k += 1
                ins.then_inc(self.s, 1)
                self.eng.wait_ge(self.s, self.base + self.k)

            def end(self):
                assert self.k == self.per, self.k

        consts_loaded = sem("consts_loaded")
        ident_made = sem("ident_made")
        exp_made = sem("exp_made")
        x_loaded = [sem(f"x_loaded{u}") for u in range(2)]
        x_free = [sem(f"x_free{u}") for u in range(2)]
        var_ready = sem("var_ready")
        sqrt_made = sem("sqrt_made")
        norm_ready = sem("norm_ready")
        h_made = sem("h_made")
        h_done = [sem(f"h_done{u}") for u in range(2)]
        h_stored = [sem(f"h_stored{u}") for u in range(2)]
        h_free = [sem(f"h_free{u}") for u in range(2)]
        pads_set = sem("pads_set")
        prep_step = sem("prep_step")
        f2_all = sem("f2_all")
        f2_turned = sem("f2_turned")
        f2_copied = sem("f2_copied")
        f2_stored = sem("f2_stored")

        x_g = x.rearrange("(g b p) f -> g p b f", b=GT, p=P)
        haug_g = haug_d.rearrange("(g b p) f -> g p b f", b=GT, p=P)

        with nc.Block() as block:
            @block.sync
            def _(sp):
                sp.dma_start(a_row[:], a.rearrange("f one -> one f").broadcast_to([P, 2 * F])).then_inc(consts_loaded, 16)
                sp.dma_start(temp_b[:], temp.rearrange("(one k) -> one k", one=1).broadcast_to([P, 5])).then_inc(consts_loaded, 16)
                with sp.Fori(0, NG // 2) as q:
                    for u in range(2):
                        sp.wait_ge(x_free[u], q + 1)
                        sp.dma_start(X[:, u], x_g[bass.ds(2 * q + u, 1)].rearrange("g p b f -> (g p) b f")).then_inc(x_loaded[u], 16)
                sp.wait_ge(f2_copied, 1)
                sp.dma_start(f2_d, f2t[:]).then_inc(f2_stored, 16)
                sp.wait_ge(f2_stored, 16)

            @block.gpsimd
            def _(pool):
                nc.gpsimd.memset(zeros[:], 0.0)
                nc.gpsimd.memset(H[:, :, :, F + 2:AUG], 0.0).then_inc(pads_set, 1)
                nc.gpsimd.iota(LIST[:], pattern=[[1, NT]], base=0, channel_multiplier=0)
                nc.gpsimd.memset(COUNT[:], NT)
                nc.gpsimd.memset(ident[:], 0.0).then_inc(ident_made, 1)
                pool.wait_ge(ident_made, 1)
                nc.gpsimd.affine_select(out=ident[:], in_=ident[:], compare_op=ALU.not_equal, fill=1.0, base=0,
                                        pattern=[[-1, P]], channel_multiplier=1).then_inc(ident_made, 1)
                for u in range(2):
                    pool.sem_inc(h_free[u], 1)
                with pool.Fori(0, NG // 2) as q:
                    for u in range(2):
                        pool.wait_ge(h_done[u], q + 1)
                        pool.dma_start(haug_g[bass.ds(2 * q + u, 1)].rearrange("g p b f -> (g p) b f"), H[:, u]).then_inc(h_stored[u], 16)
                    for u in range(2):
                        pool.wait_ge(h_stored[u], 16 * q + 16)
                        pool.sem_inc(h_free[u], 1)

            @block.scalar
            def _(act):
                act.wait_ge(consts_loaded, 32)
                nc.scalar.activation(coe[:], temp_b[:], ACT.Exp, scale=-1.0).then_inc(exp_made, 1)
                for u in range(2):
                    act.sem_inc(x_free[u], 1)
                with act.Fori(0, NG // 2) as q:
                    for u in range(2):
                        act.wait_ge(var_ready, 2 * q + u + 1)
                        nc.scalar.activation(sm[:, 1], sm[:, 0], ACT.Sqrt).then_inc(sqrt_made, 1)
                        act.wait_ge(norm_ready, 2 * q + u + 1)
                        act.wait_ge(h_free[u], q + 1)
                        for b in range(GT):
                            ins = nc.scalar.activation(H[:, u, b, 0:F], X[:, u, b], ACT.Relu,
                                                       bias=sm[:, 5, b:b + 1], scale=sm[:, 4, b:b + 1])
                        ins.then_inc(h_made, 1)
                        act.drain().then_inc(x_free[u], 1)
                act.wait_ge(f2_turned, 1)
                nc.scalar.copy(f2t[:], MISC[0:NT, :]).then_inc(f2_copied, 1)

            @block.tensor
            def _(pe):
                pe.wait_ge(ident_made, 2)
                pe.wait_ge(f2_all, 1)
                nc.tensor.transpose(MISC[0:NT, :], F2[:], ident[:]).then_inc(f2_turned, 1)

            @block.vector
            def _(dve):
                PER = 9
                dve.wait_ge(exp_made, 1)
                step = Steps(dve, prep_step, 0, 4)
                step(nc.vector.tensor_scalar_add(one_m[:], coe[:], 1.0))
                step(nc.vector.reciprocal(coe[:], one_m[:]))
                step(nc.vector.tensor_scalar(one_m[:], coe[:], -1.0, 1.0, ALU.mult, ALU.add))
                nc.vector.tensor_tensor(one_c0[:, 0:1], one_m[:, 1:2], coe[:, 0:1], ALU.mult)
                step(nc.vector.tensor_tensor(one_c0[:, 1:2], one_m[:, 1:2], one_m[:, 0:1], ALU.mult))
                step.end()
                dve.wait_ge(pads_set, 1)
                with dve.Fori(0, NG // 2) as q:
                    for u in range(2):
                        step = Steps(dve, prep_step, 4 + (2 * q + u) * PER, PER)
                        dve.wait_ge(x_loaded[u], 16 * q + 16)
                        for b in range(GT):
                            ins = nc.vector.bn_stats(st[:, b, :], X[:, u, b])
                        step(ins)
                        nc.vector.tensor_tensor(mv[:, 0], st[:, :, 1], st[:, :, 4], ALU.add)
                        nc.vector.tensor_tensor(mv[:, 1], st[:, :, 1], st[:, :, 4], ALU.subtract)
                        step(nc.vector.tensor_tensor(mv[:, 2], st[:, :, 2], st[:, :, 5], ALU.add))
                        nc.vector.tensor_tensor(mv[:, 3], mv[:, 1], mv[:, 1], ALU.mult)
                        step(nc.vector.tensor_scalar(mv[:, 4], mv[:, 2], 1.0 / F, EPS, ALU.mult, ALU.add))
                        nc.vector.scalar_tensor_tensor(sm[:, 0], mv[:, 3], 0.25, mv[:, 4], ALU.mult,
                                                       ALU.add).then_inc(var_ready, 1)
                        dve.wait_ge(sqrt_made, 2 * q + u + 1)
                        step(nc.vector.reciprocal(sm[:, 2], sm[:, 1]))
                        step(nc.vector.tensor_tensor(sm[:, 3], sm[:, 2], sm[:, 0], ALU.mult))
                        step(nc.vector.tensor_tensor(sm[:, 2], sm[:, 3], sm[:, 1], ALU.add))
                        step(nc.vector.reciprocal(sm[:, 3], sm[:, 2]))
                        step(nc.vector.tensor_scalar_mul(sm[:, 4], sm[:, 3], 2.0))
                        nc.vector.scalar_tensor_tensor(sm[:, 5], mv[:, 0], -0.5, sm[:, 4], ALU.mult,
                                                       ALU.mult).then_inc(norm_ready, 1)
                        dve.wait_ge(h_made, 2 * q + u + 1)
                        for b in range(GT):
                            for k, (col, w) in enumerate(((COL_F1, a_row[:, 0:F]), (COL_F2, a_row[:, F:2 * F]))):
                                ins = nc.vector.scalar_tensor_tensor(jnk[:, 2 * b + k], H[:, u, b, 0:F], 1.0, w, ALU.mult, ALU.mult,
                                                                     accum_out=H[:, u, b, col:col + 1])
                        step(ins)
                        g8 = (2 * q + u) * GT
                        nc.vector.tensor_copy(F1[:, bass.ds(g8, GT)], H[:, u, :, COL_F1])
                        nc.vector.tensor_copy(F2[:, bass.ds(g8, GT)], H[:, u, :, COL_F2]).then_inc(h_done[u], 1)
                        step.end()
                dve.drain().then_inc(f2_all, 1)

        def feat_steps(step, acc, hrow, invz, rows, coef, t, ft):
            step(nc.vector.tensor_tensor(coef, one_m[:, 2:3], rows, ALU.subtract))
            step(nc.vector.tensor_scalar(t, hrow, coef, None, ALU.mult))
            step(nc.vector.scalar_tensor_tensor(t, acc, invz, t, ALU.mult, ALU.add))
            step(nc.vector.tensor_scalar(ft, t, -THRESH, THRESH, ALU.max, ALU.min))
            return nc.vector.tensor_tensor(ft, t, ft, ALU.subtract)

        f2b_loaded = sem("f2b_loaded")
        a_loaded = sem("a_loaded")
        a_free = sem("a_free")
        hb_loaded = [sem(f"hb_loaded{u}") for u in range(2)]
        mm_done = [sem(f"mm_done{u}") for u in range(2)]
        sc_ready = [sem(f"sc_ready{u}") for u in range(2)]
        sc_free = [sem(f"sc_free{u}") for u in range(2)]
        att_step = sem("att_step")
        max_ready = sem("max_ready")
        pc_ready = [sem(f"pc_ready{u}") for u in range(2)]
        sq_done = [sem(f"sq_done{u}") for u in range(2)]
        tp_done = [sem(f"tp_done{u}") for u in range(2)]
        pt_ready = [sem(f"pt_ready{u}") for u in range(2)]
        pt_stored = [sem(f"pt_stored{u}") for u in range(2)]
        pt_free = [sem(f"pt_free{u}") for u in range(2)]
        acc_ready = sem("acc_ready")
        acc_free = sem("acc_free")
        d_step = sem("d_step")
        feat_ready = sem("feat_ready")
        feat_stored = sem("feat_stored")
        feat_free = sem("feat_free")

        haug_c = haug_d.rearrange("(c b p) f -> c p b f", b=CB, p=P)
        feat_c = feat_d.rearrange("(c b p) f -> c p b f", b=CB, p=P)

        def rows_of(dram, d, w):
            return dram[bass.ds(d * P, P), 0:w]

        def each_dense(eng, body):
            count = eng.value_load(COUNT[0:1, 0:1], min_val=0, max_val=NT)
            with eng.If(count > 0):
                with eng.Fori(0, count) as n:
                    body(n)
            with eng.Else():
                eng.nop()

        def tile_of(eng, n):
            return eng.value_load(LIST[0:1, bass.ds(n, 1)], min_val=0, max_val=NT - 1)

        with nc.Block() as block:
            @block.sync
            def _(sp):
                def body(n):
                    d = tile_of(sp, n)
                    sp.wait_ge(a_free, n + 1)
                    sp.dma_start(A, adj[bass.ds(d * P, P), :]).then_inc(a_loaded, 16)
                    sp.wait_ge(feat_free, n + 1)
                    sp.dma_start(HT, haug_d[bass.ds(d * P, P), :]).then_inc(a_loaded, 16)
                    with sp.Fori(0, CP) as c2:
                        for u in range(2):
                            sp.wait_ge(mm_done[u], n * CP + c2 + 1)
                            sp.dma_start(HB[:, u], haug_c[bass.ds(2 * c2 + u, 1)].rearrange("c p b f -> (c p) b f")).then_inc(hb_loaded[u], 16)
                sp.dma_start(F2B, f2_d.rearrange("t p -> (t p)").rearrange("(one n) -> one n", one=1).broadcast_to([P, N])).then_inc(f2b_loaded, 16)
                each_dense(sp, body)

            @block.scalar
            def _(act):
                act.wait_ge(f2b_loaded, 16)
                act.sem_inc(a_free, 1)

                def body(n):
                    d = tile_of(act, n)
                    with act.Fori(0, CP) as c2:
                        for u in range(2):
                            act.wait_ge(sc_free[u], n * CP + c2 + 1)
                            act.wait_ge(f2b_loaded, 16)
                            nc.scalar.activation(SC[:, u], F2B[:, bass.ds((2 * c2 + u) * CW, CW)], ACT.Identity,
                                                 bias=F1[:, bass.ds(d, 1)]).then_inc(sc_ready[u], 1)
                    act.wait_ge(max_ready, n + 1)
                    with act.Fori(0, CP) as c2:
                        for u in range(2):
                            act.wait_ge(pt_free[u], n * CP + c2 + 1)
                            act.wait_ge(f2b_loaded, 16)
                            nc.scalar.activation(PC[:, u], A[:, bass.ds((2 * c2 + u) * CW, CW)], ACT.Exp,
                                                 bias=dsm[:, 1:2], accum_out=Zc[:, bass.ds(2 * c2 + u, 1)]).then_inc(pc_ready[u], 1)
                            act.wait_ge(pc_ready[u], n * CP + c2 + 1)
                            nc.scalar.activation(SC[:, u], PC[:, u], ACT.Square,
                                                 accum_out=Qc[:, bass.ds(2 * c2 + u, 1)]).then_inc(sq_done[u], 1)
                    act.drain().then_inc(a_free, 1)
                each_dense(act, body)

            @block.vector
            def _(dve):
                for u in range(2):
                    dve.sem_inc(sc_free[u], 1)
                    dve.sem_inc(pt_free[u], 1)
                dve.sem_inc(acc_free, 1)
                dve.sem_inc(feat_free, 1)

                def body(n):
                    d = tile_of(dve, n)
                    with dve.Fori(0, CP) as c2:
                        for u in range(2):
                            dve.wait_ge(a_loaded, 32 * n + 32)
                            cc = n * CP + c2
                            step = Steps(dve, att_step, (cc * 2 + u) * 3, 3)
                            Ac = A[:, bass.ds((2 * c2 + u) * CW, CW)]
                            step(nc.vector.tensor_scalar(Ac, Ac, 0.0, 2 * NEG, ALU.is_gt, ALU.mult))
                            dve.wait_ge(sc_ready[u], cc + 1)
                            step(nc.vector.scalar_tensor_tensor(SC[:, u], SC[:, u], ALPHA, SC[:, u], ALU.mult, ALU.max))
                            step(nc.vector.scalar_tensor_tensor(Ac, Ac, -NEG, SC[:, u], ALU.add, ALU.min))
                            dve.sem_inc(sc_free[u], 1)
                            step.end()
                    step = Steps(dve, d_step, n * 11, 11)
                    step(nc.vector.reduce_max(dsm[:, 0:1], A, AX.X))
                    nc.vector.tensor_scalar_mul(dsm[:, 1:2], dsm[:, 0:1], -1.0).then_inc(max_ready, 1)
                    with dve.Fori(0, CP) as c2:
                        for u in range(2):
                            cc = n * CP + c2
                            dve.wait_ge(tp_done[u], cc + 1)
                            nc.vector.tensor_copy(PT[:, u], TP[u][:]).then_inc(pt_ready[u], 1)
                    for u in range(2):
                        dve.wait_ge(sq_done[u], (n + 1) * CP)
                    step(nc.vector.reduce_sum(dsm[:, 2:3], Zc[:], AX.X))
                    step(nc.vector.reciprocal(dsm[:, 3:4], dsm[:, 2:3]))
                    step(nc.vector.reduce_sum(dsm[:, 4:5], Qc[:], AX.X))
                    step(nc.vector.tensor_tensor(dsm[:, 5:6], dsm[:, 4:5], dsm[:, 3:4], ALU.mult))
                    step(nc.vector.scalar_tensor_tensor(dsm[:, 6:7], dsm[:, 5:6], 0.5, dsm[:, 3:4], ALU.mult, ALU.mult))
                    nc.vector.tensor_copy(INVZ[:, bass.ds(d, 1)], dsm[:, 3:4])
                    step(nc.vector.tensor_copy(ROWS[:, bass.ds(d, 1)], dsm[:, 6:7]))
                    dve.wait_ge(acc_ready, n + 1)
                    last = feat_steps(step, ACC[:], HT[:, 0:F], dsm[:, 3:4], dsm[:, 6:7], dsm[:, 7:8], T0[:], FT[:])
                    last.then_inc(feat_ready, 1)
                    dve.wait_ge(feat_ready, n + 1)
                    dve.sem_inc(acc_free, 1)
                    step.end()
                each_dense(dve, body)

            @block.gpsimd
            def _(pool):
                def body(n):
                    d = tile_of(pool, n)
                    with pool.Fori(0, CP) as c2:
                        for u in range(2):
                            cc = n * CP + c2
                            pool.wait_ge(pt_ready[u], cc + 1)
                            pool.dma_start(pt_d[bass.ds(n, 1), :, bass.ds((2 * c2 + u) * CW, CW)].rearrange("n p c -> (n p) c"),
                                           PT[:, u]).then_inc(pt_stored[u], 16)
                            pool.wait_ge(pt_stored[u], cc * 16 + 16)
                            pool.wait_ge(mm_done[u], cc + 2)
                            pool.sem_inc(pt_free[u], 1)
                    pool.wait_ge(feat_ready, n + 1)
                    pool.dma_start(feat_d[bass.ds(d * P, P), :], FT[:]).then_inc(feat_stored, 16)
                    pool.wait_ge(feat_stored, 16 * n + 16)
                    pool.sem_inc(feat_free, 1)
                each_dense(pool, body)

            @block.tensor
            def _(pe):
                for u in range(2):
                    pe.sem_inc(mm_done[u], 1)

                def body(n):
                    pe.wait_ge(acc_free, n + 1)
                    nc.tensor.matmul(ACC[:], zeros[:], a_row[:, 0:F], start=True, stop=False)
                    with pe.Fori(0, CP) as c2:
                        for u in range(2):
                            cc = n * CP + c2
                            pe.wait_ge(pc_ready[u], cc + 1)
                            for b in range(CB):
                                ins = nc.tensor.transpose(TP[u][:, b * P:(b + 1) * P], PC[:, u, b * P:(b + 1) * P], ident[:])
                            ins.then_inc(tp_done[u], 1)
                            pe.wait_ge(pt_ready[u], cc + 1)
                            pe.wait_ge(hb_loaded[u], 16 * cc + 16)
                            for b in range(CB):
                                ins = nc.tensor.matmul(ACC[:], PT[:, u, b * P:(b + 1) * P], HB[:, u, b, 0:F], start=False, stop=False)
                            ins.then_inc(mm_done[u], 1)
                    nc.tensor.matmul(ACC[:], zeros[:], a_row[:, 0:F], start=False, stop=True).then_inc(acc_ready, 1)
                each_dense(pe, body)

        p2_loaded = [sem(f"p2_loaded{u}") for u in range(2)]
        p2_used = [sem(f"p2_used{u}") for u in range(2)]
        own_loaded = sem("own_loaded")
        acc2_ready = sem("acc2_ready")
        acc2_free = sem("acc2_free")
        e_step = sem("e_step")
        out_ready = sem("out_ready")
        out_stored = sem("out_stored")
        own_free = sem("own_free")

        def out_steps(step, acc, xr, fr, h0r, invz, rows, s, t, o):
            step(nc.vector.scalar_tensor_tensor(s[:, 0:1], rows, coe[:, 1:2], one_c0[:, 0:1], ALU.mult, ALU.add))
            step(nc.vector.tensor_tensor(s[:, 1:2], s[:, 0:1], coe[:, 3:4], ALU.mult))
            step(nc.vector.tensor_tensor(s[:, 1:2], coe[:, 1:2], s[:, 1:2], ALU.subtract))
            step(nc.vector.tensor_tensor(s[:, 1:2], s[:, 1:2], invz, ALU.mult))
            step(nc.vector.scalar_tensor_tensor(t, fr, s[:, 0:1], xr, ALU.mult, ALU.add))
            step(nc.vector.scalar_tensor_tensor(t, h0r, one_c0[:, 1:2], t, ALU.mult, ALU.add))
            return nc.vector.scalar_tensor_tensor(o, acc, s[:, 1:2], t, ALU.mult, ALU.add)

        with nc.Block() as block:
            @block.sync
            def _(sp):
                def body(n):
                    d = tile_of(sp, n)
                    sp.wait_ge(own_free, n + 1)
                    sp.dma_start(XT[:], x[bass.ds(d * P, P), :]).then_inc(own_loaded, 16)
                    sp.dma_start(H0T[:], h0[bass.ds(d * P, P), :]).then_inc(own_loaded, 16)
                    sp.dma_start(T2[:], feat_d[bass.ds(d * P, P), :]).then_inc(own_loaded, 16)
                    with sp.Fori(0, CP) as c2:
                        for u in range(2):
                            sp.wait_ge(p2_used[u], n * CP + c2 + 1)
                            sp.dma_start(PT[:, u], pt_d[bass.ds(n, 1), :, bass.ds((2 * c2 + u) * CW, CW)].rearrange("n p c -> (n p) c")).then_inc(p2_loaded[u], 16)
                            sp.dma_start(FB[:, u], feat_c[bass.ds(2 * c2 + u, 1)].rearrange("c p b f -> (c p) b f")).then_inc(p2_loaded[u], 16)
                each_dense(sp, body)

            @block.tensor
            def _(pe):
                for u in range(2):
                    pe.sem_inc(p2_used[u], 1)

                def body(n):
                    pe.wait_ge(acc2_free, n + 1)
                    nc.tensor.matmul(ACC[:], zeros[:], a_row[:, 0:F], start=True, stop=False)
                    with pe.Fori(0, CP) as c2:
                        for u in range(2):
                            cc = n * CP + c2
                            pe.wait_ge(p2_loaded[u], 32 * cc + 32)
                            for b in range(CB):
                                ins = nc.tensor.matmul(ACC[:], PT[:, u, b * P:(b + 1) * P], FB[:, u, b], start=False, stop=False)
                            ins.then_inc(p2_used[u], 1)
                    nc.tensor.matmul(ACC[:], zeros[:], a_row[:, 0:F], start=False, stop=True).then_inc(acc2_ready, 1)
                each_dense(pe, body)

            @block.vector
            def _(dve):
                dve.sem_inc(acc2_free, 1)
                dve.sem_inc(own_free, 1)

                def body(n):
                    d = tile_of(dve, n)
                    step = Steps(dve, e_step, n * 7, 7)
                    nc.vector.tensor_copy(dsm[:, 3:4], INVZ[:, bass.ds(d, 1)])
                    step(nc.vector.tensor_copy(dsm[:, 6:7], ROWS[:, bass.ds(d, 1)]))
                    dve.wait_ge(own_loaded, 48 * n + 48)
                    dve.wait_ge(acc2_ready, n + 1)
                    last = out_steps(step, ACC[:], XT[:], T2[:], H0T[:], dsm[:, 3:4], dsm[:, 6:7], dsm[:, 8:10], T0[:], OT[:])
                    last.then_inc(out_ready, 1)
                    dve.wait_ge(out_ready, n + 1)
                    dve.sem_inc(acc2_free, 1)
                    step.end()
                each_dense(dve, body)

            @block.gpsimd
            def _(pool):
                def body(n):
                    d = tile_of(pool, n)
                    pool.wait_ge(out_ready, n + 1)
                    pool.dma_start(out[bass.ds(d * P, P), :], OT[:]).then_inc(out_stored, 16)
                    pool.wait_ge(out_stored, 16 * n + 16)
                    pool.sem_inc(own_free, 1)
                each_dense(pool, body)


_INS = ['x', 'adj', 'L0_gnn_h0', 'L0_gnn_a', 'L0_gnn_temp']
_OUTS = [((8192, 256), 'float32')]


def kernel(**inputs):
    import numpy as _np
    import concourse.bacc as _bacc
    from concourse import mybir as _mybir
    from concourse.bass_utils import run_bass_kernel_spmd as _run

    nc = _bacc.Bacc("TRN2", target_bir_lowering=False, num_devices=1)
    arrays, args = {}, []
    for name in _INS:
        v = _np.ascontiguousarray(inputs[name])
        arrays[f"in_{name}_dram"] = v
        args.append(nc.dram_tensor(f"in_{name}_dram", v.shape, _mybir.dt.from_np(v.dtype), kind="ExternalInput").ap())
    for i, (shape, dtype) in enumerate(_OUTS):
        dt = _mybir.dt.from_np(_np.dtype(dtype))
        args.append(nc.dram_tensor(f"out_{i}_dram", shape, dt, kind="ExternalOutput").ap())
    adj_preln_kernel(nc, *args)
    r = _run(nc, [arrays], core_ids=[0])
    return r.results[0]["out_0_dram"]
```

```python
import concourse.bass as bass
from concourse import mybir
from contextlib import ExitStack

fp32 = mybir.dt.float32
i32 = mybir.dt.int32
bf16 = mybir.dt.bfloat16
ALU = mybir.AluOpType
ACT = mybir.ActivationFunctionType
AX = mybir.AxisListType


def adj_preln_kernel(nc, x, adj, h0, a, temp, out):
    N, F = x.shape
    P = 128
    NT = N // P
    AUG = F + 8
    COL_F2, COL_F1 = F, F + 1
    GT = 8
    NG = NT // GT
    CW = 1024
    CB = CW // P
    CP = N // CW // 2
    K = 24
    KG = 4
    RANGES = [r for r in ((0, 64, 2), (128, 128, 1), (256, 256, 1), (512, 512, 3), (2048, 1024, 2), (4096, 2048, 2)) if r[0] < N]
    NR = sum(n for _, _, n in RANGES)
    DENSE = 1000.0
    NEG = 9.0e15
    ALPHA = 0.2
    THRESH = 1e-6
    EPS = 1e-5

    ctx = ExitStack()
    with ctx:
        def sb(name, shape, dt=fp32):
            return ctx.enter_context(nc.sbuf_tensor(name, shape, dt))

        def pb(name, shape, dt=fp32):
            return ctx.enter_context(nc.psum_tensor(name, shape, dt))

        def sem(name):
            return ctx.enter_context(nc.semaphore(name))

        haug_d = nc.dram_tensor("haug_d", (N, AUG), fp32).ap()
        feat_d = nc.dram_tensor("feat_d", (N, F), fp32).ap()
        f2_d = nc.dram_tensor("f2_d", (NT, P), fp32).ap()
        pt_d = nc.dram_tensor("pt_d", (NT, P, N), fp32).ap()

        ident = sb("ident", [P, P])
        zeros = sb("zeros", [P, P])
        a_row = sb("a_row", [P, 2 * F])
        temp_b = sb("temp_b", [P, 5])
        coe = sb("coe", [P, 5])
        one_m = sb("one_m", [P, 5])
        one_c0 = sb("one_c0", [P, 2])
        F1 = sb("F1", [P, NT])
        F2 = sb("F2", [P, NT])
        INVZ = sb("INVZ", [P, NT])
        ROWS = sb("ROWS", [P, NT])
        IDX = sb("IDX", [P, NT, K], i32)
        WGT = sb("WGT", [P, NT, K])
        CTL = sb("CTL", [1, NT, 2], i32)
        KTOP = sb("KTOP", [1, NT])
        LIST = sb("LIST", [1, NT], i32)
        COUNT = sb("COUNT", [1, 1], i32)

        R = sb("R", [P, 13 * 1024])
        W2 = sb("W2", [P, 2, N])
        X = R[:, 0:2 * GT * F].rearrange("p (u b f) -> p u b f", u=2, b=GT)
        HO = 2 * GT * F
        H = R[:, HO:HO + 2 * GT * AUG].rearrange("p (u b f) -> p u b f", u=2, b=GT)
        SC = R[:, 0:2 * CW].rearrange("p (u c) -> p u c", u=2)
        PC = R[:, 2 * CW:4 * CW].rearrange("p (u c) -> p u c", u=2)
        PT = R[:, 4 * CW:6 * CW].rearrange("p (u c) -> p u c", u=2)
        HB = R[:, 6 * CW:6 * CW + 2 * CB * AUG].rearrange("p (u b f) -> p u b f", u=2, b=CB)
        FB = R[:, 6 * CW:6 * CW + 2 * CB * F].rearrange("p (u b f) -> p u b f", u=2, b=CB)
        EO = 6 * CW + 2 * CB * AUG
        HT = R[:, EO:EO + AUG]
        A = W2[:, 0, :]
        F2B = W2[:, 1, :]

        G = R[:, 0:2 * K * AUG].rearrange("p (u k f) -> p u k f", u=2, k=K)
        SGW = N + 8 * NR
        SG = sb("SG", [P, 2, SGW], bf16)
        DG = sb("DG", [P, 2, K, P])
        HTS = sb("HTS", [P, 2, AUG])
        FTS = sb("FTS", [P, 2, F])
        XTS = sb("XTS", [P, 2, F])
        H0S = sb("H0S", [P, 2, F])
        OTS = sb("OTS", [P, 2, F])
        ONES8 = sb("ONES8", [P, 8])
        WIDTH = sb("WIDTH", [P, NR, 8])
        FIRST = sb("FIRST", [P, NR, 8])
        MI = sb("MI", [P, 2, NR, 8], mybir.dt.uint32)
        VAL = sb("VAL", [P, NR, 8])
        KEY = sb("KEY", [P, 2, NR, 8])
        TOP = sb("TOP", [P, K])
        PAD = sb("PAD", [P, K])
        PEN = sb("PEN", [P, 2, K])
        IDS = sb("IDS", [P, 2, K], i32)
        SCR = sb("SCR", [P, 2, K])
        WS = sb("WS", [P, 2, K])
        WQ = sb("WQ", [P, K])
        cnt = sb("cnt", [P, 8])
        msm = sb("msm", [P, 2, 8])
        ksm = sb("ksm", [1, 8])
        kcc = sb("kcc", [1, 2, 2])
        pair0 = sb("pair0", [1, 2, K // 2])
        psc = sb("psc", [1, K // 2])
        back = sb("back", [1, NT])
        ONE_R = sb("ONE_R", [1, NT])
        lkey = sb("lkey", [1, 3, NT])

        st = sb("st", [P, GT, 6])
        mv = sb("mv", [P, 5, GT])
        sm = sb("sm", [P, 6, GT])
        jnk = SG[:].rearrange("p u w -> p (u w)")[:, 0:2 * GT * F].rearrange("p (b f) -> p b f", f=F)
        f2t = sb("f2t", [NT, P])
        dsm = sb("dsm", [P, 16])
        Zc = sb("Zc", [P, 2 * CP])
        Qc = sb("Qc", [P, 2 * CP])
        T0 = sb("T0", [P, F])
        XT, H0T, OT, FT, T2 = XTS[:, 0], H0S[:, 0], OTS[:, 0], FTS[:, 0], FTS[:, 1]

        TP = [pb(f"TP{u}", [P, CW]) for u in range(2)]
        ACCS = [pb(f"ACC{u}", [P, F]) for u in range(2)]
        ACC = ACCS[0]
        MISC = pb("MISC", [P, P])

        class Steps:

            def __init__(self, eng, s, base, per):
                self.eng, self.s, self.base, self.per, self.k = eng, s, base, per, 0

            def mark(self, ins):
                self.k += 1
                ins.then_inc(self.s, 1)

            def need(self):
                self.eng.wait_ge(self.s, self.base + self.k)

            def __call__(self, ins):
                self.mark(ins)
                self.need()

            def end(self):
                assert self.k == self.per, self.k

        consts_loaded = sem("consts_loaded")
        ident_made = sem("ident_made")
        exp_made = sem("exp_made")
        x_loaded = [sem(f"x_loaded{u}") for u in range(2)]
        x_free = [sem(f"x_free{u}") for u in range(2)]
        var_ready = sem("var_ready")
        sqrt_made = sem("sqrt_made")
        norm_ready = sem("norm_ready")
        h_made = sem("h_made")
        h_done = [sem(f"h_done{u}") for u in range(2)]
        h_stored = [sem(f"h_stored{u}") for u in range(2)]
        h_free = [sem(f"h_free{u}") for u in range(2)]
        pads_set = sem("pads_set")
        prep_step = sem("prep_step")
        f2_all = sem("f2_all")
        f2_turned = sem("f2_turned")
        f2_copied = sem("f2_copied")
        f2_stored = sem("f2_stored")
        adj_loaded = [sem(f"adj_loaded{u}") for u in range(2)]

        x_g = x.rearrange("(g b p) f -> g p b f", b=GT, p=P)
        haug_g = haug_d.rearrange("(g b p) f -> g p b f", b=GT, p=P)

        with nc.Block() as block:
            @block.sync
            def _(sp):
                sp.dma_start(a_row[:], a.rearrange("f one -> one f").broadcast_to([P, 2 * F])).then_inc(consts_loaded, 16)
                sp.dma_start(temp_b[:], temp.rearrange("(one k) -> one k", one=1).broadcast_to([P, 5])).then_inc(consts_loaded, 16)
                with sp.Fori(0, NG // 2) as q:
                    for u in range(2):
                        sp.wait_ge(x_free[u], q + 1)
                        sp.dma_start(X[:, u], x_g[bass.ds(2 * q + u, 1)].rearrange("g p b f -> (g p) b f")).then_inc(x_loaded[u], 16)
                for u in range(2):
                    sp.dma_start(W2[:, u], adj[u * P:(u + 1) * P, :]).then_inc(adj_loaded[u], 16)
                sp.wait_ge(f2_copied, 1)
                sp.dma_start(f2_d, f2t[:]).then_inc(f2_stored, 16)
                sp.wait_ge(f2_stored, 16)

            @block.gpsimd
            def _(pool):
                nc.gpsimd.memset(zeros[:], 0.0)
                nc.gpsimd.memset(H[:, :, :, F + 2:AUG], 0.0).then_inc(pads_set, 1)
                nc.gpsimd.memset(R[:, HO + 2 * GT * AUG:], 0.0)
                nc.gpsimd.memset(ONES8[:], 1.0)
                nc.gpsimd.memset(ONE_R[:], 1.0)
                nc.gpsimd.memset(pair0[:, 1], 1.0)
                nc.gpsimd.memset(kcc[:], 0.0)
                for i in range(K // 2):
                    nc.gpsimd.memset(pair0[:, 0, i:i + 1], 2.0 * i)
                r = 0
                for first, width, n in RANGES:
                    for i in range(n):
                        nc.gpsimd.memset(WIDTH[:, r], float(width))
                        nc.gpsimd.memset(FIRST[:, r], float(first + i * width + 1))
                        r += 1
                nc.gpsimd.iota(back[:], pattern=[[-1, NT]], base=NT, channel_multiplier=0, allow_small_or_imprecise_dtypes=True)
                nc.gpsimd.memset(ident[:], 0.0).then_inc(ident_made, 1)
                pool.wait_ge(ident_made, 1)
                nc.gpsimd.affine_select(out=ident[:], in_=ident[:], compare_op=ALU.not_equal, fill=1.0, base=0,
                                        pattern=[[-1, P]], channel_multiplier=1).then_inc(ident_made, 1)
                for u in range(2):
                    pool.sem_inc(h_free[u], 1)
                with pool.Fori(0, NG // 2) as q:
                    for u in range(2):
                        pool.wait_ge(h_done[u], q + 1)
                        pool.dma_start(haug_g[bass.ds(2 * q + u, 1)].rearrange("g p b f -> (g p) b f"), H[:, u]).then_inc(h_stored[u], 16)
                    for u in range(2):
                        pool.wait_ge(h_stored[u], 16 * q + 16)
                        pool.sem_inc(h_free[u], 1)

            @block.scalar
            def _(act):
                act.wait_ge(consts_loaded, 32)
                nc.scalar.activation(coe[:], temp_b[:], ACT.Exp, scale=-1.0).then_inc(exp_made, 1)
                for u in range(2):
                    act.sem_inc(x_free[u], 1)
                with act.Fori(0, NG // 2) as q:
                    for u in range(2):
                        act.wait_ge(var_ready, 2 * q + u + 1)
                        nc.scalar.activation(sm[:, 1], sm[:, 0], ACT.Sqrt).then_inc(sqrt_made, 1)
                        act.wait_ge(norm_ready, 2 * q + u + 1)
                        act.wait_ge(h_free[u], q + 1)
                        for b in range(GT):
                            ins = nc.scalar.activation(H[:, u, b, 0:F], X[:, u, b], ACT.Relu,
                                                       bias=sm[:, 5, b:b + 1], scale=sm[:, 4, b:b + 1])
                        ins.then_inc(h_made, 1)
                        act.drain().then_inc(x_free[u], 1)
                act.wait_ge(f2_turned, 1)
                nc.scalar.copy(f2t[:], MISC[0:NT, :]).then_inc(f2_copied, 1)

            @block.tensor
            def _(pe):
                pe.wait_ge(ident_made, 2)
                pe.wait_ge(f2_all, 1)
                nc.tensor.transpose(MISC[0:NT, :], F2[:], ident[:]).then_inc(f2_turned, 1)

            @block.vector
            def _(dve):
                PER = 9
                dve.wait_ge(exp_made, 1)
                step = Steps(dve, prep_step, 0, 4)
                step(nc.vector.tensor_scalar_add(one_m[:], coe[:], 1.0))
                step(nc.vector.reciprocal(coe[:], one_m[:]))
                step(nc.vector.tensor_scalar(one_m[:], coe[:], -1.0, 1.0, ALU.mult, ALU.add))
                nc.vector.tensor_tensor(one_c0[:, 0:1], one_m[:, 1:2], coe[:, 0:1], ALU.mult)
                step(nc.vector.tensor_tensor(one_c0[:, 1:2], one_m[:, 1:2], one_m[:, 0:1], ALU.mult))
                step.end()
                dve.wait_ge(pads_set, 1)
                with dve.Fori(0, NG // 2) as q:
                    for u in range(2):
                        step = Steps(dve, prep_step, 4 + (2 * q + u) * PER, PER)
                        dve.wait_ge(x_loaded[u], 16 * q + 16)
                        for b in range(GT):
                            ins = nc.vector.bn_stats(st[:, b, :], X[:, u, b])
                        step(ins)
                        nc.vector.tensor_tensor(mv[:, 0], st[:, :, 1], st[:, :, 4], ALU.add)
                        nc.vector.tensor_tensor(mv[:, 1], st[:, :, 1], st[:, :, 4], ALU.subtract)
                        step(nc.vector.tensor_tensor(mv[:, 2], st[:, :, 2], st[:, :, 5], ALU.add))
                        nc.vector.tensor_tensor(mv[:, 3], mv[:, 1], mv[:, 1], ALU.mult)
                        step(nc.vector.tensor_scalar(mv[:, 4], mv[:, 2], 1.0 / F, EPS, ALU.mult, ALU.add))
                        nc.vector.scalar_tensor_tensor(sm[:, 0], mv[:, 3], 0.25, mv[:, 4], ALU.mult,
                                                       ALU.add).then_inc(var_ready, 1)
                        dve.wait_ge(sqrt_made, 2 * q + u + 1)
                        step(nc.vector.reciprocal(sm[:, 2], sm[:, 1]))
                        step(nc.vector.tensor_tensor(sm[:, 3], sm[:, 2], sm[:, 0], ALU.mult))
                        step(nc.vector.tensor_tensor(sm[:, 2], sm[:, 3], sm[:, 1], ALU.add))
                        step(nc.vector.reciprocal(sm[:, 3], sm[:, 2]))
                        step(nc.vector.tensor_scalar_mul(sm[:, 4], sm[:, 3], 2.0))
                        nc.vector.scalar_tensor_tensor(sm[:, 5], mv[:, 0], -0.5, sm[:, 4], ALU.mult,
                                                       ALU.mult).then_inc(norm_ready, 1)
                        dve.wait_ge(h_made, 2 * q + u + 1)
                        for b in range(GT):
                            for k, (col, w) in enumerate(((COL_F1, a_row[:, 0:F]), (COL_F2, a_row[:, F:2 * F]))):
                                ins = nc.vector.scalar_tensor_tensor(jnk[:, 2 * b + k], H[:, u, b, 0:F], 1.0, w, ALU.mult, ALU.mult,
                                                                     accum_out=H[:, u, b, col:col + 1])
                        step(ins)
                        g8 = (2 * q + u) * GT
                        nc.vector.tensor_copy(F1[:, bass.ds(g8, GT)], H[:, u, :, COL_F1])
                        nc.vector.tensor_copy(F2[:, bass.ds(g8, GT)], H[:, u, :, COL_F2]).then_inc(h_done[u], 1)
                        step.end()
                dve.drain().then_inc(f2_all, 1)

        def feat_steps(step, acc, hrow, invz, rows, coef, t, ft):
            step(nc.vector.tensor_tensor(coef, one_m[:, 2:3], rows, ALU.subtract))
            step(nc.vector.tensor_scalar(t, hrow, coef, None, ALU.mult))
            step(nc.vector.scalar_tensor_tensor(t, acc, invz, t, ALU.mult, ALU.add))
            step(nc.vector.tensor_scalar(ft, t, -THRESH, THRESH, ALU.max, ALU.min))
            return nc.vector.tensor_tensor(ft, t, ft, ALU.subtract)


        adj_free = [sem(f"adj_free{u}") for u in range(2)]
        sg_ready = [sem(f"sg_ready{u}") for u in range(2)]
        sg_free = [sem(f"sg_free{u}") for u in range(2)]
        own_h_loaded = [sem(f"own_h_loaded{u}") for u in range(2)]
        own_h_free = [sem(f"own_h_free{u}") for u in range(2)]
        ones_set = sem("ones_set")
        s1_step = sem("s1_step")
        search_done = sem("search_done")
        counts_ready = sem("counts_ready")
        counts_turned = sem("counts_turned")
        ctl_ready = sem("ctl_ready")
        gathered = [sem(f"gathered{u}") for u in range(2)]
        g_free = [sem(f"g_free{u}") for u in range(2)]
        s2_step = sem("s2_step")
        top_ready = sem("top_ready")
        w_made = sem("w_made")
        sums_ready = sem("sums_ready")
        diag_ready = sem("diag_ready")
        prod_ready = sem("prod_ready")
        s3_step = sem("s3_step")
        sfeat_ready = [sem(f"sfeat_ready{u}") for u in range(2)]
        sfeat_stored = [sem(f"sfeat_stored{u}") for u in range(2)]
        sfeat_free = [sem(f"sfeat_free{u}") for u in range(2)]

        def offsets():
            r, out = 0, []
            for first, width, n in RANGES:
                for i in range(n):
                    at = first + i * width
                    out.append((r, at, width, at + 8 * r))
                    r += 1
            return out

        def tile_loop(eng, body, lag):
            peeled = lag + lag % 2
            for t in range(peeled):
                body((t, t // 2, t % 2), lambda l: t >= l)
            with eng.Fori(peeled // 2, NT // 2) as q:
                for u in range(2):
                    body((2 * q + u, q, u), lambda l: True)
            for t in range(NT, NT + lag):
                body((t, t // 2, t % 2), lambda l: t - l < NT)

        def before(turn, l):
            t, q, u = turn
            return t - l, q - (l + 1 - u) // 2, (u + l) % 2

        def gather_slots(pool, t, u, table, w, gathered):
            slots = pool.value_load(CTL[0:1, bass.ds(t, 1), 0:1].rearrange("a b c -> a (b c)"), min_val=1, max_val=K)

            def pair(s):
                for k in (s, s + 1):
                    pool.indirect_dma_start(out=G[:, u, k, 0:w], out_offset=None, in_=table,
                                            in_offset=bass.IndirectOffsetOnAxis(ap=IDS[:, u, k:k + 1], axis=0),
                                            bounds_check=N - 1, oob_is_err=False).then_inc(gathered[u], 16)
            pair(0)
            for s in range(2, K, 2):
                with pool.If(slots > s):
                    pair(s)
                with pool.Else():
                    pool.nop()

        def diagonals(act, t, u, done):
            slots = act.value_load(CTL[0:1, bass.ds(t, 1), 0:1].rearrange("a b c -> a (b c)"), min_val=1, max_val=K)

            def group(g):
                for k in range(g * KG, (g + 1) * KG):
                    nc.scalar.mul(DG[:, u, k], ident[:], WS[:, u, k:k + 1])
            group(0)
            for g in range(1, K // KG):
                with act.If(slots > g * KG):
                    group(g)
                with act.Else():
                    act.nop()
            act.drain().then_inc(done, 1)

        def slots_of(eng, t):
            return eng.value_load(CTL[0:1, bass.ds(t, 1), 0:1].rearrange("a b c -> a (b c)"), min_val=1, max_val=K)

        def arrival_of(eng, t):
            return eng.value_load(CTL[0:1, bass.ds(t, 1), 1:2].rearrange("a b c -> a (b c)"), min_val=32, max_val=16 * K * NT)

        def products(pe, t, u, done):
            nc.tensor.matmul(ACCS[u][:], zeros[:], a_row[:, 0:F], start=True, stop=False)
            slots = slots_of(pe, t)

            def group(g):
                for k in range(g * KG, (g + 1) * KG):
                    ins = nc.tensor.matmul(ACCS[u][:], DG[:, u, k], G[:, u, k, 0:F], start=False, stop=(k == KG - 1))
                return ins
            for g in range(1, K // KG):
                with pe.If(slots > g * KG):
                    group(g)
                with pe.Else():
                    pe.nop()
            group(0).then_inc(done, 1)

        with nc.Block() as block:
            @block.sync
            def _(sp):
                def own_rows(t, q, u):
                    sp.wait_ge(own_h_free[u], q + 1)
                    sp.dma_start(HTS[:, u], haug_d[bass.ds(t * P, P), :]).then_inc(own_h_loaded[u], 16)

                def body(turn, live):
                    t, q, u = turn
                    if live(0) and not (isinstance(t, int) and t < 2):
                        sp.wait_ge(adj_free[u], q)
                        sp.dma_start(W2[:, u], adj[bass.ds(t * P, P), :]).then_inc(adj_loaded[u], 16)
                    if live(6):
                        own_rows(*before(turn, 6))
                tile_loop(sp, body, 6)

            @block.scalar
            def _(act):
                def signs(t, q, u):
                    act.wait_ge(adj_loaded[u], 16 * q + 16)
                    act.wait_ge(sg_free[u], q + 1)
                    r = 0
                    for first, width, n in RANGES:
                        at = first + 8 * r
                        dst = SG[:, u, at:at + n * (width + 8)].rearrange("p (n w) -> p n w", n=n)[:, :, 0:width]
                        src = W2[:, u, first:first + n * width].rearrange("p (n w) -> p n w", n=n)
                        ins = nc.scalar.activation(dst, src, ACT.Sign)
                        r += n
                    ins.then_inc(sg_ready[u], 1)
                    act.wait_ge(sg_ready[u], q + 1)
                    act.sem_inc(adj_free[u], 1)

                def weights(t, q, u):
                    act.wait_ge(top_ready, t + 1)
                    act.wait_ge(prod_ready, t + 1)
                    nc.scalar.activation(WS[:, u], SCR[:, u], ACT.Exp, bias=msm[:, u, 1:2],
                                         accum_out=msm[:, u, 2:3]).then_inc(w_made, 1)
                    act.wait_ge(w_made, t + 1)
                    nc.scalar.copy(WGT[:, bass.ds(t, 1)].rearrange("p a k -> p (a k)"), WS[:, u])
                    nc.scalar.activation(WQ[:], WS[:, u], ACT.Square, accum_out=msm[:, u, 3:4]).then_inc(sums_ready, 1)
                    act.wait_ge(sums_ready, t + 1)
                    diagonals(act, t, u, diag_ready)

                def body(turn, live):
                    if live(0):
                        signs(*turn)
                    if live(4):
                        weights(*before(turn, 4))
                tile_loop(act, body, 4)

            @block.gpsimd
            def _(pool):
                for u in range(2):
                    pool.sem_inc(sfeat_free[u], 1)

                def store(t, q, u):
                    pool.wait_ge(sfeat_ready[u], q + 2)
                    pool.dma_start(feat_d[bass.ds(t * P, P), :], FTS[:, u]).then_inc(sfeat_stored[u], 16)
                    pool.wait_ge(sfeat_stored[u], 16 * q + 16)
                    pool.sem_inc(sfeat_free[u], 1)

                def body(turn, live):
                    t, q, u = turn
                    if live(3):
                        store(*before(turn, 3))
                    if live(0):
                        pool.wait_ge(ctl_ready, t + 1)
                        pool.wait_ge(prod_ready, t + 1)
                        gather_slots(pool, t, u, haug_d, AUG, gathered)
                tile_loop(pool, body, 3)

            @block.tensor
            def _(pe):
                pe.sem_inc(prod_ready, 2)

                def turn_counts(t):
                    pe.wait_ge(counts_ready, t + 1)
                    nc.tensor.matmul(MISC[0:1, :], cnt[:, 4:5], ident[:], start=True, stop=True).then_inc(counts_turned, 1)

                def product(t, q, u):
                    pe.wait_ge(diag_ready, t + 1)
                    pe.wait_ge(sfeat_ready[u], q + 1)
                    products(pe, t, u, prod_ready)

                def body(turn, live):
                    if live(1):
                        turn_counts(before(turn, 1)[0])
                    if live(3):
                        product(*before(turn, 3))
                tile_loop(pe, body, 3)

            @block.vector
            def _(dve):
                for r, at, width, off in offsets():
                    for u in range(2):
                        nc.vector.memset(SG[:, u, off + width:off + width + 8], 1.0)
                dve.drain().then_inc(ones_set, 1)
                dve.wait_ge(ones_set, 1)
                for u in range(2):
                    dve.sem_inc(sg_free[u], 1)
                    dve.sem_inc(own_h_free[u], 1)
                    dve.sem_inc(sfeat_ready[u], 1)

                def body(turn, live):
                    on, on_a, on_b, on_c = (live(l) for l in (0, 1, 3, 4))
                    t, q, u = turn
                    ta, qa, ua = before(turn, 1)
                    tb, qb, ub = before(turn, 3)
                    tc, qc, uc = before(turn, 4)
                    A_, B_, C_ = (Steps(dve, s_, t_ * n_, n_) for s_, t_, n_ in ((s1_step, ta, 12), (s2_step, tb, 4), (s3_step, tc, 7)))
                    m = msm[:, ub]
                    s = msm[:, uc]
                    if on:
                        dve.wait_ge(sg_ready[u], q + 1)
                        nc.vector.memset(cnt[:, 5:6], 0.0)

                    def look(*ranges):
                        if on:
                            for r in ranges:
                                if r < NR:
                                    _, _, width, off = offsets()[r]
                                    ins = nc.vector.max_index(out=MI[:, u, r], in_max=ONES8[:], in_values=SG[:, u, off:off + width + 8])
                                    if r == min(6, NR - 1):
                                        ins.then_inc(search_done, 1)

                    def pads(x_, y_):
                        nc.vector.tensor_scalar(PEN[:, ua, x_:y_], TOP[:, x_:y_], 0.0, 2 * NEG, ALU.is_gt, ALU.mult)
                        return nc.vector.tensor_scalar(PAD[:, x_:y_], TOP[:, x_:y_], 0.0, float(2 * N), ALU.is_equal, ALU.mult)

                    if on_b:
                        dve.wait_ge(gathered[ub], arrival_of(dve, tb))
                        B_.mark(nc.vector.tensor_scalar(SCR[:, ub], G[:, ub, :, COL_F2], F1[:, bass.ds(tb, 1)], None, ALU.add))
                    look(0)
                    if on_a:
                        dve.wait_ge(search_done, ta + 1)
                        nc.vector.scalar_tensor_tensor(VAL[:], MI[:, ua], 1.0, WIDTH[:], ALU.mult, ALU.is_lt, accum_out=cnt[:, 0:1])
                        A_.mark(nc.vector.tensor_tensor(KEY[:, 0], MI[:, ua], FIRST[:], ALU.add))
                    look(1)
                    if on_b:
                        B_.need()
                        B_.mark(nc.vector.scalar_tensor_tensor(SCR[:, ub], SCR[:, ub], ALPHA, SCR[:, ub], ALU.mult, ALU.max))
                    look(7)
                    if on_a:
                        A_.need()
                        nc.vector.reduce_max(cnt[:, 1:2], VAL[:, :, 7], AX.X)
                        nc.vector.tensor_scalar(cnt[:, 2:3], cnt[:, 0:1], 0.0, DENSE, ALU.is_equal, ALU.mult)
                        A_.mark(nc.vector.tensor_tensor(KEY[:, 1], KEY[:, 0], VAL[:], ALU.mult))
                    if on_b:
                        B_.need()
                        B_.mark(nc.vector.scalar_tensor_tensor(SCR[:, ub], PEN[:, ub], -NEG, SCR[:, ub], ALU.add, ALU.min))
                    if on_c:
                        dve.wait_ge(sums_ready, tc + 1)
                        C_.mark(nc.vector.reciprocal(s[:, 4:5], s[:, 2:3]))
                    look(8)
                    if on_a:
                        A_.need()
                        nc.vector.scalar_tensor_tensor(cnt[:, 3:4], cnt[:, 1:2], DENSE, cnt[:, 0:1], ALU.mult, ALU.max)
                        A_.mark(nc.vector.max(TOP[:, 0:8], KEY[:, 1]))
                    if on_b:
                        B_.need()
                        B_.mark(nc.vector.reduce_max(m[:, 0:1], SCR[:, ub], AX.X))
                    if on_c:
                        C_.need()
                        C_.mark(nc.vector.tensor_tensor(s[:, 5:6], s[:, 3:4], s[:, 4:5], ALU.mult))
                    look(9)
                    if on_a:
                        A_.need()
                        nc.vector.tensor_tensor(cnt[:, 4:5], cnt[:, 3:4], cnt[:, 2:3], ALU.max).then_inc(counts_ready, 1)
                        A_.mark(nc.vector.match_replace(KEY[:, 0], TOP[:, 0:8], KEY[:, 1], 0.0))
                    if on_b:
                        B_.need()
                        nc.vector.tensor_scalar_mul(m[:, 1:2], m[:, 0:1], -1.0).then_inc(top_ready, 1)
                    if on_c:
                        C_.need()
                        C_.mark(nc.vector.scalar_tensor_tensor(s[:, 6:7], s[:, 5:6], 0.5, s[:, 4:5], ALU.mult, ALU.mult))
                    look(2)
                    if on_a:
                        A_.need()
                        pads(0, 8)
                        A_.mark(nc.vector.max(TOP[:, 8:16], KEY[:, 0]))
                    if on_c:
                        C_.need()
                        nc.vector.tensor_copy(INVZ[:, bass.ds(tc, 1)], s[:, 4:5])
                        nc.vector.tensor_copy(ROWS[:, bass.ds(tc, 1)], s[:, 6:7])
                        C_.mark(nc.vector.tensor_tensor(s[:, 7:8], one_m[:, 2:3], s[:, 6:7], ALU.subtract))
                    look(10)
                    if on_c:
                        C_.need()
                        dve.wait_ge(own_h_loaded[uc], 16 * qc + 16)
                        C_.mark(nc.vector.tensor_scalar(T0[:], HTS[:, uc, 0:F], s[:, 7:8], None, ALU.mult))
                    if on_a:
                        A_.need()
                        pads(8, 16)
                        A_.mark(nc.vector.match_replace(KEY[:, 1], TOP[:, 8:16], KEY[:, 0], 0.0))
                    look(3)
                    if on_a:
                        dve.wait_ge(counts_turned, ta + 1)
                        nc.vector.reduce_max(ksm[:, 0:1], MISC[0:1, :], AX.X)
                        A_.need()
                        nc.vector.memset(cnt[:, 6:7], 0.0)
                        A_.mark(nc.vector.max(TOP[:, 16:24], KEY[:, 1]))
                    if on_c:
                        C_.need()
                        dve.wait_ge(prod_ready, tc + 3)
                        C_.mark(nc.vector.scalar_tensor_tensor(T0[:], ACCS[uc][:], s[:, 4:5], T0[:], ALU.mult, ALU.add))
                    look(4)
                    if on_a:
                        A_.need()
                        nc.vector.tensor_copy(KTOP[:, bass.ds(ta, 1)], ksm[:, 0:1])
                        nc.vector.tensor_scalar(ksm[:, 1:2], ksm[:, 0:1], float(K), None, ALU.is_le)
                        A_.mark(pads(16, 24))
                    if on_c:
                        C_.need()
                        dve.wait_ge(sfeat_free[uc], qc + 1)
                        C_.mark(nc.vector.tensor_scalar(FTS[:, uc], T0[:], -THRESH, THRESH, ALU.max, ALU.min))
                    look(5)
                    if on_a:
                        A_.need()
                        A_.mark(nc.vector.tensor_scalar(kcc[:, ua, 0:1], ksm[:, 0:1], ksm[:, 1:2], 1.0, ALU.mult, ALU.max))
                        nc.vector.scalar_tensor_tensor(IDS[:, ua], TOP[:], -1.0, PAD[:], ALU.add, ALU.add)
                        nc.vector.scalar_tensor_tensor(IDX[:, bass.ds(ta, 1)].rearrange("p a k -> p (a k)"), TOP[:], -1.0, PAD[:], ALU.add, ALU.add)
                        A_.need()
                        A_.mark(nc.vector.scalar_tensor_tensor(psc[:], pair0[:, 0], kcc[:, ua, 0:1], pair0[:, 1], ALU.is_lt, ALU.mult,
                                                               accum_out=ksm[:, 2:3]))
                    look(6)
                    if on:
                        dve.wait_ge(search_done, t + 1)
                        dve.sem_inc(sg_free[u], 1)
                    if on_a:
                        A_.need()
                        A_.mark(nc.vector.scalar_tensor_tensor(kcc[:, ua, 1:2], ksm[:, 2:3], 32.0, kcc[:, ua, 1:2], ALU.mult, ALU.add))
                    if on_c:
                        C_.need()
                        nc.vector.tensor_tensor(FTS[:, uc], T0[:], FTS[:, uc], ALU.subtract).then_inc(sfeat_ready[uc], 1)
                        dve.sem_inc(own_h_free[uc], 1)
                    if on_a:
                        A_.need()
                        A_.mark(nc.vector.tensor_copy(CTL[:, bass.ds(ta, 1)].rearrange("a b c -> a (b c)"), kcc[:, ua]))
                        A_.need()
                        dve.sem_inc(ctl_ready, 1)
                        A_.end()
                    if on_b:
                        B_.end()
                    if on_c:
                        assert C_.k == 7, C_.k
                        C_.end()
                tile_loop(dve, body, 4)

                list_step = sem("list_step")
                step = Steps(dve, list_step, 0, 3 + 2 * (NT // 8))
                step(nc.vector.scalar_tensor_tensor(lkey[:, 0], KTOP[:], float(K), ONE_R[:], ALU.is_gt, ALU.mult, accum_out=ksm[:, 3:4]))
                nc.vector.tensor_copy(COUNT[:], ksm[:, 3:4])
                step(nc.vector.tensor_tensor(lkey[:, 1], lkey[:, 0], back[:], ALU.mult))
                for i in range(NT // 8):
                    a_, b_ = 1 - i % 2, i % 2
                    step(nc.vector.max(lkey[:, 2, 8 * i:8 * i + 8], lkey[:, a_]))
                    step(nc.vector.match_replace(lkey[:, b_], lkey[:, 2, 8 * i:8 * i + 8], lkey[:, a_], 0.0))
                step(nc.vector.tensor_scalar(lkey[:, 0], lkey[:, 2], -1.0, float(NT), ALU.mult, ALU.add))
                nc.vector.tensor_scalar(LIST[:], lkey[:, 0], float(NT - 1), None, ALU.min)
                step.end()

        f2b_loaded = sem("f2b_loaded")
        a_loaded = sem("a_loaded")
        a_free = sem("a_free")
        hb_loaded = [sem(f"hb_loaded{u}") for u in range(2)]
        mm_done = [sem(f"mm_done{u}") for u in range(2)]
        sc_ready = [sem(f"sc_ready{u}") for u in range(2)]
        sc_free = [sem(f"sc_free{u}") for u in range(2)]
        att_step = sem("att_step")
        max_ready = sem("max_ready")
        pc_ready = [sem(f"pc_ready{u}") for u in range(2)]
        sq_done = [sem(f"sq_done{u}") for u in range(2)]
        tp_done = [sem(f"tp_done{u}") for u in range(2)]
        pt_ready = [sem(f"pt_ready{u}") for u in range(2)]
        pt_stored = [sem(f"pt_stored{u}") for u in range(2)]
        pt_free = [sem(f"pt_free{u}") for u in range(2)]
        acc_ready = sem("acc_ready")
        acc_free = sem("acc_free")
        d_step = sem("d_step")
        feat_ready = sem("feat_ready")
        feat_stored = sem("feat_stored")
        feat_free = sem("feat_free")

        haug_c = haug_d.rearrange("(c b p) f -> c p b f", b=CB, p=P)
        feat_c = feat_d.rearrange("(c b p) f -> c p b f", b=CB, p=P)

        def rows_of(dram, d, w):
            return dram[bass.ds(d * P, P), 0:w]

        def each_dense(eng, body):
            count = eng.value_load(COUNT[0:1, 0:1], min_val=0, max_val=NT)
            with eng.If(count > 0):
                with eng.Fori(0, count) as n:
                    body(n)
            with eng.Else():
                eng.nop()

        def tile_of(eng, n):
            return eng.value_load(LIST[0:1, bass.ds(n, 1)], min_val=0, max_val=NT - 1)

        with nc.Block() as block:
            @block.sync
            def _(sp):
                def body(n):
                    d = tile_of(sp, n)
                    sp.wait_ge(a_free, n + 1)
                    sp.dma_start(A, adj[bass.ds(d * P, P), :]).then_inc(a_loaded, 16)
                    sp.wait_ge(feat_free, n + 1)
                    sp.dma_start(HT, haug_d[bass.ds(d * P, P), :]).then_inc(a_loaded, 16)
                    with sp.Fori(0, CP) as c2:
                        for u in range(2):
                            sp.wait_ge(mm_done[u], n * CP + c2 + 1)
                            sp.dma_start(HB[:, u], haug_c[bass.ds(2 * c2 + u, 1)].rearrange("c p b f -> (c p) b f")).then_inc(hb_loaded[u], 16)
                sp.dma_start(F2B, f2_d.rearrange("t p -> (t p)").rearrange("(one n) -> one n", one=1).broadcast_to([P, N])).then_inc(f2b_loaded, 16)
                each_dense(sp, body)

            @block.scalar
            def _(act):
                act.wait_ge(f2b_loaded, 16)
                act.sem_inc(a_free, 1)

                def body(n):
                    d = tile_of(act, n)
                    with act.Fori(0, CP) as c2:
                        for u in range(2):
                            act.wait_ge(sc_free[u], n * CP + c2 + 1)
                            act.wait_ge(f2b_loaded, 16)
                            nc.scalar.activation(SC[:, u], F2B[:, bass.ds((2 * c2 + u) * CW, CW)], ACT.Identity,
                                                 bias=F1[:, bass.ds(d, 1)]).then_inc(sc_ready[u], 1)
                    act.wait_ge(max_ready, n + 1)
                    with act.Fori(0, CP) as c2:
                        for u in range(2):
                            act.wait_ge(tp_done[u], n * CP + c2 + 1)
                            act.wait_ge(f2b_loaded, 16)
                            nc.scalar.activation(PC[:, u], A[:, bass.ds((2 * c2 + u) * CW, CW)], ACT.Exp,
                                                 bias=dsm[:, 1:2], accum_out=Zc[:, bass.ds(2 * c2 + u, 1)]).then_inc(pc_ready[u], 1)
                            act.wait_ge(pc_ready[u], n * CP + c2 + 1)
                            nc.scalar.activation(SC[:, u], PC[:, u], ACT.Square,
                                                 accum_out=Qc[:, bass.ds(2 * c2 + u, 1)]).then_inc(sq_done[u], 1)
                    act.drain().then_inc(a_free, 1)
                each_dense(act, body)

            @block.vector
            def _(dve):
                for u in range(2):
                    dve.sem_inc(sc_free[u], 1)
                    dve.sem_inc(pt_free[u], 1)
                dve.sem_inc(acc_free, 1)
                dve.sem_inc(feat_free, 1)

                def body(n):
                    d = tile_of(dve, n)
                    with dve.Fori(0, CP) as c2:
                        for u in range(2):
                            dve.wait_ge(a_loaded, 32 * n + 32)
                            cc = n * CP + c2
                            step = Steps(dve, att_step, (cc * 2 + u) * 3, 3)
                            Ac = A[:, bass.ds((2 * c2 + u) * CW, CW)]
                            step(nc.vector.tensor_scalar(Ac, Ac, 0.0, 2 * NEG, ALU.is_gt, ALU.mult))
                            dve.wait_ge(sc_ready[u], cc + 1)
                            step(nc.vector.scalar_tensor_tensor(SC[:, u], SC[:, u], ALPHA, SC[:, u], ALU.mult, ALU.max))
                            step(nc.vector.scalar_tensor_tensor(Ac, Ac, -NEG, SC[:, u], ALU.add, ALU.min))
                            dve.sem_inc(sc_free[u], 1)
                            step.end()
                    step = Steps(dve, d_step, n * 11, 11)
                    step(nc.vector.reduce_max(dsm[:, 0:1], A, AX.X))
                    nc.vector.tensor_scalar_mul(dsm[:, 1:2], dsm[:, 0:1], -1.0).then_inc(max_ready, 1)
                    with dve.Fori(0, CP) as c2:
                        for u in range(2):
                            cc = n * CP + c2
                            dve.wait_ge(pt_free[u], cc + 1)
                            dve.wait_ge(tp_done[u], cc + 2)
                            nc.vector.tensor_copy(PT[:, u], TP[u][:]).then_inc(pt_ready[u], 1)
                    for u in range(2):
                        dve.wait_ge(sq_done[u], (n + 1) * CP)
                    step(nc.vector.reduce_sum(dsm[:, 2:3], Zc[:], AX.X))
                    step(nc.vector.reciprocal(dsm[:, 3:4], dsm[:, 2:3]))
                    step(nc.vector.reduce_sum(dsm[:, 4:5], Qc[:], AX.X))
                    step(nc.vector.tensor_tensor(dsm[:, 5:6], dsm[:, 4:5], dsm[:, 3:4], ALU.mult))
                    step(nc.vector.scalar_tensor_tensor(dsm[:, 6:7], dsm[:, 5:6], 0.5, dsm[:, 3:4], ALU.mult, ALU.mult))
                    nc.vector.tensor_copy(INVZ[:, bass.ds(d, 1)], dsm[:, 3:4])
                    step(nc.vector.tensor_copy(ROWS[:, bass.ds(d, 1)], dsm[:, 6:7]))
                    dve.wait_ge(acc_ready, n + 1)
                    last = feat_steps(step, ACC[:], HT[:, 0:F], dsm[:, 3:4], dsm[:, 6:7], dsm[:, 7:8], T0[:], FT)
                    last.then_inc(feat_ready, 1)
                    dve.wait_ge(feat_ready, n + 1)
                    dve.sem_inc(acc_free, 1)
                    step.end()
                each_dense(dve, body)

            @block.gpsimd
            def _(pool):
                def body(n):
                    d = tile_of(pool, n)
                    with pool.Fori(0, CP) as c2:
                        for u in range(2):
                            cc = n * CP + c2
                            pool.wait_ge(pt_ready[u], cc + 1)
                            pool.dma_start(pt_d[bass.ds(n, 1), :, bass.ds((2 * c2 + u) * CW, CW)].rearrange("n p c -> (n p) c"),
                                           PT[:, u]).then_inc(pt_stored[u], 16)
                            pool.wait_ge(pt_stored[u], cc * 16 + 16)
                            pool.wait_ge(mm_done[u], cc + 2)
                            pool.sem_inc(pt_free[u], 1)
                    pool.wait_ge(feat_ready, n + 1)
                    pool.dma_start(feat_d[bass.ds(d * P, P), :], FT).then_inc(feat_stored, 16)
                    pool.wait_ge(feat_stored, 16 * n + 16)
                    pool.sem_inc(feat_free, 1)
                each_dense(pool, body)

            @block.tensor
            def _(pe):
                for u in range(2):
                    pe.sem_inc(mm_done[u], 1)
                    pe.sem_inc(tp_done[u], 1)

                def body(n):
                    pe.wait_ge(acc_free, n + 1)
                    nc.tensor.matmul(ACC[:], zeros[:], a_row[:, 0:F], start=True, stop=False)
                    with pe.Fori(0, CP) as c2:
                        for u in range(2):
                            cc = n * CP + c2
                            pe.wait_ge(pc_ready[u], cc + 1)
                            for b in range(CB):
                                ins = nc.tensor.transpose(TP[u][:, b * P:(b + 1) * P], PC[:, u, b * P:(b + 1) * P], ident[:])
                            ins.then_inc(tp_done[u], 1)
                            pe.wait_ge(pt_ready[u], cc + 1)
                            pe.wait_ge(hb_loaded[u], 16 * cc + 16)
                            for b in range(CB):
                                ins = nc.tensor.matmul(ACC[:], PT[:, u, b * P:(b + 1) * P], HB[:, u, b, 0:F], start=False, stop=False)
                            ins.then_inc(mm_done[u], 1)
                    nc.tensor.matmul(ACC[:], zeros[:], a_row[:, 0:F], start=False, stop=True).then_inc(acc_ready, 1)
                each_dense(pe, body)

        def out_steps(step, acc, xr, fr, h0r, invz, rows, s, t, o, products=None):
            step(nc.vector.scalar_tensor_tensor(s[:, 0:1], rows, coe[:, 1:2], one_c0[:, 0:1], ALU.mult, ALU.add))
            step(nc.vector.tensor_tensor(s[:, 1:2], s[:, 0:1], coe[:, 3:4], ALU.mult))
            step(nc.vector.tensor_tensor(s[:, 1:2], coe[:, 1:2], s[:, 1:2], ALU.subtract))
            step(nc.vector.tensor_tensor(s[:, 1:2], s[:, 1:2], invz, ALU.mult))
            step(nc.vector.scalar_tensor_tensor(t, fr, s[:, 0:1], xr, ALU.mult, ALU.add))
            step(nc.vector.scalar_tensor_tensor(t, h0r, one_c0[:, 1:2], t, ALU.mult, ALU.add))
            if products:
                products[2].wait_ge(products[0], products[1])
            return nc.vector.scalar_tensor_tensor(o, acc, s[:, 1:2], t, ALU.mult, ALU.add)

        t2_loaded = [sem(f"t2_loaded{u}") for u in range(2)]
        t2_free = [sem(f"t2_free{u}") for u in range(2)]
        staged = sem("staged")
        gathered2 = [sem(f"gathered2{u}") for u in range(2)]
        diag2_ready = sem("diag2_ready")
        prod2_ready = sem("prod2_ready")
        s4_step = sem("s4_step")
        sout_ready = [sem(f"sout_ready{u}") for u in range(2)]
        sout_free = [sem(f"sout_free{u}") for u in range(2)]
        sout_stored = [sem(f"sout_stored{u}") for u in range(2)]

        with nc.Block() as block:
            @block.sync
            def _(sp):
                def store(t, q, u):
                    sp.wait_ge(sout_ready[u], q + 2)
                    sp.dma_start(out[bass.ds(t * P, P), :], OTS[:, u]).then_inc(sout_stored[u], 16)
                    sp.wait_ge(sout_stored[u], 16 * q + 16)
                    sp.sem_inc(sout_free[u], 1)

                def body(turn, live):
                    t, q, u = turn
                    if live(2):
                        store(*before(turn, 2))
                    if not live(0):
                        return
                    sp.dma_start(XTS[:, u], x[bass.ds(t * P, P), :]).then_inc(t2_loaded[u], 16)
                    sp.dma_start(H0S[:, u], h0[bass.ds(t * P, P), :]).then_inc(t2_loaded[u], 16)
                    sp.dma_start(FTS[:, u], feat_d[bass.ds(t * P, P), :]).then_inc(t2_loaded[u], 16)
                for u in range(2):
                    sp.sem_inc(sout_free[u], 1)
                tile_loop(sp, body, 2)

            @block.scalar
            def _(act):
                def body(turn, live):
                    t, q, u = turn
                    act.wait_ge(staged, t + 1)
                    act.wait_ge(prod2_ready, t + 1)
                    diagonals(act, t, u, diag2_ready)
                tile_loop(act, body, 0)

            @block.gpsimd
            def _(pool):
                def body(turn, live):
                    t, q, u = turn
                    pool.wait_ge(staged, t + 1)
                    pool.wait_ge(prod2_ready, t + 1)
                    gather_slots(pool, t, u, feat_d, F, gathered2)
                tile_loop(pool, body, 0)

            @block.tensor
            def _(pe):
                def body(turn, live):
                    t, q, u = turn
                    pe.wait_ge(gathered2[u], arrival_of(pe, t))
                    pe.wait_ge(diag2_ready, t + 1)
                    pe.wait_ge(sout_ready[u], q + 1)
                    products(pe, t, u, prod2_ready)
                pe.sem_inc(prod2_ready, 2)
                tile_loop(pe, body, 0)

            @block.vector
            def _(dve):
                def stage(t, q, u):
                    dve.wait_ge(prod2_ready, t + 1)
                    nc.vector.tensor_copy(IDS[:, u], IDX[:, bass.ds(t, 1)].rearrange("p a k -> p (a k)"))
                    nc.vector.tensor_copy(WS[:, u], WGT[:, bass.ds(t, 1)].rearrange("p a k -> p (a k)")).then_inc(staged, 1)

                def finish(t, q, u):
                    step = Steps(dve, s4_step, t * 7, 7)
                    s = msm[:, u]
                    nc.vector.tensor_copy(s[:, 4:5], INVZ[:, bass.ds(t, 1)])
                    step(nc.vector.tensor_copy(s[:, 6:7], ROWS[:, bass.ds(t, 1)]))
                    dve.wait_ge(t2_loaded[u], 48 * q + 48)
                    dve.wait_ge(sout_free[u], q + 1)
                    last = out_steps(step, ACCS[u][:], XTS[:, u], FTS[:, u], H0S[:, u], s[:, 4:5], s[:, 6:7], s[:, 0:2], T0[:], OTS[:, u],
                                     (prod2_ready, t + 3, dve))
                    last.then_inc(sout_ready[u], 1)
                    step.end()

                def body(turn, live):
                    if live(1):
                        stage(*turn) if live(0) else None
                        finish(*before(turn, 1))
                    else:
                        stage(*turn)
                for u in range(2):
                    dve.sem_inc(sout_ready[u], 1)
                tile_loop(dve, body, 1)

        p2_loaded = [sem(f"p2_loaded{u}") for u in range(2)]
        p2_used = [sem(f"p2_used{u}") for u in range(2)]
        own_loaded = sem("own_loaded")
        acc2_ready = sem("acc2_ready")
        acc2_free = sem("acc2_free")
        e_step = sem("e_step")
        out_ready = sem("out_ready")
        out_stored = sem("out_stored")
        own_free = sem("own_free")

        with nc.Block() as block:
            @block.sync
            def _(sp):
                def body(n):
                    d = tile_of(sp, n)
                    sp.wait_ge(own_free, n + 1)
                    sp.dma_start(XT, x[bass.ds(d * P, P), :]).then_inc(own_loaded, 16)
                    sp.dma_start(H0T, h0[bass.ds(d * P, P), :]).then_inc(own_loaded, 16)
                    sp.dma_start(T2, feat_d[bass.ds(d * P, P), :]).then_inc(own_loaded, 16)
                    with sp.Fori(0, CP) as c2:
                        for u in range(2):
                            sp.wait_ge(p2_used[u], n * CP + c2 + 1)
                            sp.dma_start(PT[:, u], pt_d[bass.ds(n, 1), :, bass.ds((2 * c2 + u) * CW, CW)].rearrange("n p c -> (n p) c")).then_inc(p2_loaded[u], 16)
                            sp.dma_start(FB[:, u], feat_c[bass.ds(2 * c2 + u, 1)].rearrange("c p b f -> (c p) b f")).then_inc(p2_loaded[u], 16)
                each_dense(sp, body)

            @block.tensor
            def _(pe):
                for u in range(2):
                    pe.sem_inc(p2_used[u], 1)

                def body(n):
                    pe.wait_ge(acc2_free, n + 1)
                    nc.tensor.matmul(ACC[:], zeros[:], a_row[:, 0:F], start=True, stop=False)
                    with pe.Fori(0, CP) as c2:
                        for u in range(2):
                            cc = n * CP + c2
                            pe.wait_ge(p2_loaded[u], 32 * cc + 32)
                            for b in range(CB):
                                ins = nc.tensor.matmul(ACC[:], PT[:, u, b * P:(b + 1) * P], FB[:, u, b], start=False, stop=False)
                            ins.then_inc(p2_used[u], 1)
                    nc.tensor.matmul(ACC[:], zeros[:], a_row[:, 0:F], start=False, stop=True).then_inc(acc2_ready, 1)
                each_dense(pe, body)

            @block.vector
            def _(dve):
                dve.sem_inc(acc2_free, 1)
                dve.sem_inc(own_free, 1)

                def body(n):
                    d = tile_of(dve, n)
                    step = Steps(dve, e_step, n * 7, 7)
                    nc.vector.tensor_copy(dsm[:, 3:4], INVZ[:, bass.ds(d, 1)])
                    step(nc.vector.tensor_copy(dsm[:, 6:7], ROWS[:, bass.ds(d, 1)]))
                    dve.wait_ge(own_loaded, 48 * n + 48)
                    dve.wait_ge(acc2_ready, n + 1)
                    last = out_steps(step, ACC[:], XT, T2, H0T, dsm[:, 3:4], dsm[:, 6:7], dsm[:, 8:10], T0[:], OT)
                    last.then_inc(out_ready, 1)
                    dve.wait_ge(out_ready, n + 1)
                    dve.sem_inc(acc2_free, 1)
                    step.end()
                each_dense(dve, body)

            @block.gpsimd
            def _(pool):
                def body(n):
                    d = tile_of(pool, n)
                    pool.wait_ge(out_ready, n + 1)
                    pool.dma_start(out[bass.ds(d * P, P), :], OT).then_inc(out_stored, 16)
                    pool.wait_ge(out_stored, 16 * n + 16)
                    pool.sem_inc(own_free, 1)
                each_dense(pool, body)


_INS = ['x', 'adj', 'L0_gnn_h0', 'L0_gnn_a', 'L0_gnn_temp']
_OUTS = [((8192, 256), 'float32')]


def kernel(**inputs):
    import numpy as _np
    import concourse.bacc as _bacc
    from concourse import mybir as _mybir
    from concourse.bass_utils import run_bass_kernel_spmd as _run

    nc = _bacc.Bacc("TRN2", target_bir_lowering=False, num_devices=1)
    arrays, args = {}, []
    for name in _INS:
        v = _np.ascontiguousarray(inputs[name])
        arrays[f"in_{name}_dram"] = v
        args.append(nc.dram_tensor(f"in_{name}_dram", v.shape, _mybir.dt.from_np(v.dtype), kind="ExternalInput").ap())
    for i, (shape, dtype) in enumerate(_OUTS):
        dt = _mybir.dt.from_np(_np.dtype(dtype))
        args.append(nc.dram_tensor(f"out_{i}_dram", shape, dt, kind="ExternalOutput").ap())
    adj_preln_kernel(nc, *args)
    r = _run(nc, [arrays], core_ids=[0])
    return r.results[0]["out_0_dram"]
```
